# Optimizing a Trainium2 kernel written in Bass

```python
import numpy as np
import jax
import jax.numpy as jnp

def _softmax(x, axis=-1):
    return jax.nn.softmax(x, axis=axis)

def _gelu(x):
    return jax.nn.gelu(x, approximate=True)

def _silu(x):
    return jax.nn.silu(x)

def _sigmoid(x):
    return jax.nn.sigmoid(x)

def _layernorm(x, axis=-1, eps=1e-05):
    m = jnp.mean(x, axis=axis, keepdims=True)
    v = jnp.var(x, axis=axis, keepdims=True)
    return (x - m) / jnp.sqrt(v + eps)

def _scatter_add(tgt, idx, src, axis=0):
    return tgt.at[idx].add(src)

def _segment_sum(src, seg, n):
    return jax.ops.segment_sum(src, seg, n)
kernel_name = 'mk_dlrm_tower_d1_rec_r8_7e560a'

def setup_inputs(seed: int=0):
    np.random.seed(seed)
    _w = jnp.asarray

    def _rec_inputs():
        import jax
        import jax.numpy as jnp
        _tk = jax.random.key(seed)
        dense_ctx = jax.random.normal(jax.random.fold_in(_tk, 190), (512, 16), jnp.float32)
        ids = jnp.stack([jax.random.randint(jax.random.fold_in(_tk, 200 + f), (512,), 0, v, jnp.int32) for f, v in enumerate([1250, 12500, 125000, 12500, 1000, 1250, 1000, 1000, 1250, 12500, 12500, 1250, 12500, 125000, 1000, 125000, 1000, 12500, 1000, 12500, 1000, 12500, 1250, 1250, 1000, 1250, 1000, 1250, 1000, 1250, 1000, 1000])], axis=1)
        tbl_0 = 0.05 * jax.random.normal(jax.random.fold_in(_tk, 500 + 0), (1250, 64), jnp.float32)
        tbl_1 = 0.05 * jax.random.normal(jax.random.fold_in(_tk, 500 + 1), (12500, 64), jnp.float32)
        tbl_2 = 0.05 * jax.random.normal(jax.random.fold_in(_tk, 500 + 2), (125000, 64), jnp.float32)
        tbl_3 = 0.05 * jax.random.normal(jax.random.fold_in(_tk, 500 + 3), (12500, 64), jnp.float32)
        tbl_4 = 0.05 * jax.random.normal(jax.random.fold_in(_tk, 500 + 4), (1000, 64), jnp.float32)
        tbl_5 = 0.05 * jax.random.normal(jax.random.fold_in(_tk, 500 + 5), (1250, 64), jnp.float32)
        tbl_6 = 0.05 * jax.random.normal(jax.random.fold_in(_tk, 500 + 6), (1000, 64), jnp.float32)
        tbl_7 = 0.05 * jax.random.normal(jax.random.fold_in(_tk, 500 + 7), (1000, 64), jnp.float32)
        tbl_8 = 0.05 * jax.random.normal(jax.random.fold_in(_tk, 500 + 8), (1250, 64), jnp.float32)
        tbl_9 = 0.05 * jax.random.normal(jax.random.fold_in(_tk, 500 + 9), (12500, 64), jnp.float32)
        tbl_10 = 0.05 * jax.random.normal(jax.random.fold_in(_tk, 500 + 10), (12500, 64), jnp.float32)
        tbl_11 = 0.05 * jax.random.normal(jax.random.fold_in(_tk, 500 + 11), (1250, 64), jnp.float32)
        tbl_12 = 0.05 * jax.random.normal(jax.random.fold_in(_tk, 500 + 12), (12500, 64), jnp.float32)
        tbl_13 = 0.05 * jax.random.normal(jax.random.fold_in(_tk, 500 + 13), (125000, 64), jnp.float32)
        tbl_14 = 0.05 * jax.random.normal(jax.random.fold_in(_tk, 500 + 14), (1000, 64), jnp.float32)
        tbl_15 = 0.05 * jax.random.normal(jax.random.fold_in(_tk, 500 + 15), (125000, 64), jnp.float32)
        tbl_16 = 0.05 * jax.random.normal(jax.random.fold_in(_tk, 500 + 16), (1000, 64), jnp.float32)
        tbl_17 = 0.05 * jax.random.normal(jax.random.fold_in(_tk, 500 + 17), (12500, 64), jnp.float32)
        tbl_18 = 0.05 * jax.random.normal(jax.random.fold_in(_tk, 500 + 18), (1000, 64), jnp.float32)
        tbl_19 = 0.05 * jax.random.normal(jax.random.fold_in(_tk, 500 + 19), (12500, 64), jnp.float32)
        tbl_20 = 0.05 * jax.random.normal(jax.random.fold_in(_tk, 500 + 20), (1000, 64), jnp.float32)
        tbl_21 = 0.05 * jax.random.normal(jax.random.fold_in(_tk, 500 + 21), (12500, 64), jnp.float32)
        tbl_22 = 0.05 * jax.random.normal(jax.random.fold_in(_tk, 500 + 22), (1250, 64), jnp.float32)
        tbl_23 = 0.05 * jax.random.normal(jax.random.fold_in(_tk, 500 + 23), (1250, 64), jnp.float32)
        tbl_24 = 0.05 * jax.random.normal(jax.random.fold_in(_tk, 500 + 24), (1000, 64), jnp.float32)
        tbl_25 = 0.05 * jax.random.normal(jax.random.fold_in(_tk, 500 + 25), (1250, 64), jnp.float32)
        tbl_26 = 0.05 * jax.random.normal(jax.random.fold_in(_tk, 500 + 26), (1000, 64), jnp.float32)
        tbl_27 = 0.05 * jax.random.normal(jax.random.fold_in(_tk, 500 + 27), (1250, 64), jnp.float32)
        tbl_28 = 0.05 * jax.random.normal(jax.random.fold_in(_tk, 500 + 28), (1000, 64), jnp.float32)
        tbl_29 = 0.05 * jax.random.normal(jax.random.fold_in(_tk, 500 + 29), (1250, 64), jnp.float32)
        tbl_30 = 0.05 * jax.random.normal(jax.random.fold_in(_tk, 500 + 30), (1000, 64), jnp.float32)
        tbl_31 = 0.05 * jax.random.normal(jax.random.fold_in(_tk, 500 + 31), (1000, 64), jnp.float32)
        _rk = jax.random.fold_in(_tk, 7)
        W_top1 = 0.0441942 * jax.random.normal(jax.random.fold_in(_tk, 801), (512, 512), jnp.float32)
        W_top2 = 0.0441942 * jax.random.normal(jax.random.fold_in(_tk, 802), (512, 256), jnp.float32)
        W_top3 = 0.0625 * jax.random.normal(jax.random.fold_in(_tk, 803), (256, 1), jnp.float32)
        b_top1 = jnp.zeros((512,), jnp.float32)
        b_top2 = jnp.zeros((256,), jnp.float32)
        return (dense_ctx, ids, tbl_0, tbl_1, tbl_2, tbl_3, tbl_4, tbl_5, tbl_6, tbl_7, tbl_8, tbl_9, tbl_10, tbl_11, tbl_12, tbl_13, tbl_14, tbl_15, tbl_16, tbl_17, tbl_18, tbl_19, tbl_20, tbl_21, tbl_22, tbl_23, tbl_24, tbl_25, tbl_26, tbl_27, tbl_28, tbl_29, tbl_30, tbl_31, W_top1, b_top1, W_top2, b_top2, W_top3)
    dense_ctx, ids, tbl_0, tbl_1, tbl_2, tbl_3, tbl_4, tbl_5, tbl_6, tbl_7, tbl_8, tbl_9, tbl_10, tbl_11, tbl_12, tbl_13, tbl_14, tbl_15, tbl_16, tbl_17, tbl_18, tbl_19, tbl_20, tbl_21, tbl_22, tbl_23, tbl_24, tbl_25, tbl_26, tbl_27, tbl_28, tbl_29, tbl_30, tbl_31, W_top1, b_top1, W_top2, b_top2, W_top3 = _rec_inputs()

    def _L0_rec_setup():
        import jax, jax.numpy as jnp
        import numpy as np
        key = jax.random.key(seed)
        k1, k2 = jax.random.split(key)
        B, F, D = (512, 32, 64)
        P = F * (F - 1) // 2
        x = jax.random.normal(k1, (B, F, D), dtype=jnp.float32)
        W = jax.random.normal(k2, (P, D, D), dtype=jnp.float32) * (1.0 / np.sqrt(D))
        return {'x': x, 'W': W}
    _L0_rec_all = _L0_rec_setup()
    _L0_rec_in = {k: v for k, v in _L0_rec_all.items() if k in ('W',)}
    del _L0_rec_all
    return {'dense_ctx': dense_ctx, 'ids': ids, 'tbl_0': tbl_0, 'tbl_1': tbl_1, 'tbl_2': tbl_2, 'tbl_3': tbl_3, 'tbl_4': tbl_4, 'tbl_5': tbl_5, 'tbl_6': tbl_6, 'tbl_7': tbl_7, 'tbl_8': tbl_8, 'tbl_9': tbl_9, 'tbl_10': tbl_10, 'tbl_11': tbl_11, 'tbl_12': tbl_12, 'tbl_13': tbl_13, 'tbl_14': tbl_14, 'tbl_15': tbl_15, 'tbl_16': tbl_16, 'tbl_17': tbl_17, 'tbl_18': tbl_18, 'tbl_19': tbl_19, 'tbl_20': tbl_20, 'tbl_21': tbl_21, 'tbl_22': tbl_22, 'tbl_23': tbl_23, 'tbl_24': tbl_24, 'tbl_25': tbl_25, 'tbl_26': tbl_26, 'tbl_27': tbl_27, 'tbl_28': tbl_28, 'tbl_29': tbl_29, 'tbl_30': tbl_30, 'tbl_31': tbl_31, 'W_top1': W_top1, 'b_top1': b_top1, 'W_top2': W_top2, 'b_top2': b_top2, 'W_top3': W_top3, 'L0_rec_W': _L0_rec_in['W']}

def reference(dense_ctx, ids, tbl_0, tbl_1, tbl_2, tbl_3, tbl_4, tbl_5, tbl_6, tbl_7, tbl_8, tbl_9, tbl_10, tbl_11, tbl_12, tbl_13, tbl_14, tbl_15, tbl_16, tbl_17, tbl_18, tbl_19, tbl_20, tbl_21, tbl_22, tbl_23, tbl_24, tbl_25, tbl_26, tbl_27, tbl_28, tbl_29, tbl_30, tbl_31, W_top1, b_top1, W_top2, b_top2, W_top3, L0_rec_W):
    import jax
    import jax.numpy as jnp

    def _L0_rec_ref(x, W):
        import jax, jax.numpy as jnp
        import numpy as np
        F = x.shape[1]
        idx_i, idx_j = np.triu_indices(F, k=1)
        xi = x[:, idx_i, :]
        xj = x[:, idx_j, :]
        left = jnp.einsum('bpd,pde->bpe', xi, W)
        out = jnp.sum(left * xj, axis=-1)
        return out
    e = jnp.stack([tbl_0[ids[:, 0]], tbl_1[ids[:, 1]], tbl_2[ids[:, 2]], tbl_3[ids[:, 3]], tbl_4[ids[:, 4]], tbl_5[ids[:, 5]], tbl_6[ids[:, 6]], tbl_7[ids[:, 7]], tbl_8[ids[:, 8]], tbl_9[ids[:, 9]], tbl_10[ids[:, 10]], tbl_11[ids[:, 11]], tbl_12[ids[:, 12]], tbl_13[ids[:, 13]], tbl_14[ids[:, 14]], tbl_15[ids[:, 15]], tbl_16[ids[:, 16]], tbl_17[ids[:, 17]], tbl_18[ids[:, 18]], tbl_19[ids[:, 19]], tbl_20[ids[:, 20]], tbl_21[ids[:, 21]], tbl_22[ids[:, 22]], tbl_23[ids[:, 23]], tbl_24[ids[:, 24]], tbl_25[ids[:, 25]], tbl_26[ids[:, 26]], tbl_27[ids[:, 27]], tbl_28[ids[:, 28]], tbl_29[ids[:, 29]], tbl_30[ids[:, 30]], tbl_31[ids[:, 31]]], axis=1)
    z = _L0_rec_ref(e, L0_rec_W)
    z = z.reshape(z.shape[0], -1)
    h = jnp.concatenate([z, dense_ctx], axis=1)
    h = jnp.maximum(h @ W_top1 + b_top1, 0.0)
    h = jnp.maximum(h @ W_top2 + b_top2, 0.0)
    y = h @ W_top3
    return y

_drawn_inputs = setup_inputs


def setup_inputs(seed=0):
    import zlib

    import numpy as np

    out = dict(_drawn_inputs(seed))
    spreads = {'b_top1': (0.0, 0.1), 'b_top2': (0.0, 0.1)}
    factors = {}
    for name, (base, spread) in spreads.items():
        noise = np.random.default_rng([zlib.crc32(name.encode()), seed]).standard_normal(out[name].shape)
        drawn = base * np.exp(spread * noise) if base else spread * noise
        out[name] = jnp.asarray(drawn.astype(out[name].dtype))
    for name, factor in factors.items():
        out[name] = (out[name] * factor).astype(out[name].dtype)
    return out
```

```python
from contextlib import ExitStack

import numpy as np

import concourse.bass as bass
from concourse import mybir

ALU = mybir.AluOpType
ACT = mybir.ActivationFunctionType
F32 = mybir.dt.float32
F32R = mybir.dt.float32r
I32 = mybir.dt.int32
U32 = mybir.dt.uint32

B, F, D = 512, 32, 64
P = 128
DENSE = 16
H1, H2 = 512, 256
BT = B // P
NP = F // 2
BANK = 512

UNITS = []
FIRST = []
for _n in range(NP):
    FIRST.append(len(UNITS))
    UNITS += [(_n, _m) for _m in range(_n)]
    if _n % 2:
        UNITS.append((_n, None))
NU = len(UNITS)
CU = 4
NC = NU // CU
CC = CU * 2 * P
UZ = NU // BT
NZ = NU // UZ

LEFT_BUFS = 3
PROD_BUFS = 4
RAW_BUFS = 3
W_BUFS = 9
STACK_BUFS = 3
ROW_BUFS = 4
DVE_CHUNKS = 15
LEAD_HI = 8
LEAD_HI_LATE = 3
LEAD_LO = 7
AHEAD = [0, 0, 0, 0, 1, 1, 4] + 9 * [6]
TURN_UNITS = 2
POOL_W = 1
POOL_X = 11
MLP_LOAD = 10


def fields_of(u, half):
    n, m = UNITS[u]
    if m is None:
        k = n - 1 + half
        return 2 * k + 1, (2 * k, None)
    return 2 * n + half, (2 * m, 2 * m + 1)


def pair_index(i, j):
    return i * F - i * (i + 1) // 2 + (j - i - 1)


def z_place(u, half):
    block = 2 * (u % UZ) + half
    return u // UZ, block % 4, block // 4


def transposes_at(n):
    return FIRST[n] - AHEAD[n]


def x_lo_at(x):
    n, h = x // 2, x % 2
    return min(transposes_at(n) + TURN_UNITS + h, FIRST[n])


def chunks_by(n, lead):
    return min(4 * (n + 1), lead + 1 + transposes_at(n) // CU, NC)


def build(nc, a):
    tables = [a[f"tbl_{f}"] for f in range(F)]
    ctx = ExitStack()
    with ctx:
        def sb(name, shape, dt=F32):
            return ctx.enter_context(nc.sbuf_tensor(name, shape, dt))

        def sem(name):
            return ctx.enter_context(nc.semaphore(name))

        ident = sb("ident", [P, P])
        selector = sb("selector", [P, 62])
        ids = sb("ids", [P, BT, F], I32)
        rows = sb("rows", [P, ROW_BUFS, BT, 2, D])
        xt = sb("xt", [P, NP, B])
        stack = sb("stack", [P, STACK_BUFS, 2, B], F32R)
        w_raw = sb("w_raw", [P, RAW_BUFS, CC])
        w_hi = sb("w_hi", [P, W_BUFS, CC], F32R)
        w_lo = sb("w_lo", [P, W_BUFS, CC], F32R)
        prod = sb("prod", [P, PROD_BUFS, 2, B])
        dense = sb("dense", [P, NZ, B])
        z = sb("z", [P, NZ, B])
        w1 = sb("w1", [P, NZ, H1])
        w2 = sb("w2", [P, H1 // P, H2])
        w3 = sb("w3", [P, H2 // P])
        b1 = sb("b1", [P, H1 // P])
        b2 = sb("b2", [P, H2 // P])
        h1 = sb("h1", [P, H1 // P, B])
        h2 = sb("h2", [P, H2 // P, B])
        y = sb("y", [1, B])

        left = ctx.enter_context(nc.psum_tensor("left", [P, LEFT_BUFS, 2, BANK], F32))
        turned = ctx.enter_context(nc.psum_tensor("turned", [P, BANK], F32))
        zsum = ctx.enter_context(nc.psum_tensor("zsum", [P, BANK], F32))
        h1_acc = [left[:, 2, 0, :], left[:, 2, 1, :], left[:, 0, 0, :], left[:, 0, 1, :]]
        h2_acc = [left[:, 1, 0, :], left[:, 1, 1, :]]
        y_acc = turned[0:1, :]

        ids_loaded = sem("ids_loaded")
        raw_loaded = [sem(f"raw_loaded{i}") for i in range(RAW_BUFS)]
        mlp_loaded = sem("mlp_loaded")
        dense_loaded = sem("dense_loaded")
        rows_loaded = [sem(f"rows_loaded{i}") for i in range(ROW_BUFS)]
        y_stored = sem("y_stored")
        ident_zero = sem("ident_zero")
        ident_ready = sem("ident_ready")
        selector_zero = sem("selector_zero")
        selector_ready = sem("selector_ready")
        dense_zero = sem("dense_zero")
        turn_done = sem("turn_done")
        x_hi_done = sem("x_hi_done")
        x_lo_done = sem("x_lo_done")
        w_hi_done = sem("w_hi_done")
        w_lo_dve = sem("w_lo_dve")
        w_lo_pool = sem("w_lo_pool")
        left_done = sem("left_done")
        prod_done = sem("prod_done")
        reduce_done = sem("reduce_done")
        z_done = sem("z_done")
        l1_done = sem("l1_done")
        h1_even = sem("h1_even")
        h1_odd = sem("h1_odd")
        l2_done = sem("l2_done")
        h2_done = sem("h2_done")
        l3_done = sem("l3_done")
        y_done = sem("y_done")

        def wait_w_lo(eng, c):
            if c < DVE_CHUNKS:
                eng.wait_ge(w_lo_dve, c + 1)
            else:
                eng.wait_ge(w_lo_pool, c - DVE_CHUNKS + 1)

        def split_w_lo(eng, c, done):
            eng.wait_ge(w_hi_done, c + 1)
            if c >= W_BUFS:
                eng.wait_ge(left_done, CU * (c - W_BUFS + 1))
            eng.tensor_tensor(w_lo[:, c % W_BUFS, :], w_raw[:, c % RAW_BUFS, :],
                              w_hi[:, c % W_BUFS, :].bitcast(F32), ALU.subtract).then_inc(done, 1)

        block = ctx.enter_context(nc.Block())

        @block.sync
        def _(sp):
            sp.dma_start(ids[:], a["ids"].rearrange("(t p) f -> p t f", p=P)).then_inc(ids_loaded, 16)
            for c in range(NC):
                if c >= RAW_BUFS:
                    wait_w_lo(sp, c - RAW_BUFS)
                for half in range(2):
                    sp.dma_start(w_raw[D * half:D * half + D, c % RAW_BUFS, :],
                                 a["pair_w"][c]).then_inc(raw_loaded[c % RAW_BUFS], 16)
                if c == MLP_LOAD:
                    sp.wait_ge(dense_zero, 1)
                    for k in range(NP):
                        t, g, q = z_place(FIRST[k | 1] + (k | 1), k % 2)
                        r = 32 * g + 2 * q + 1
                        sp.dma_start(dense[r:r + 1, t, :], a["dense_t"][k:k + 1, :]).then_inc(dense_loaded, 16)
                    for dst, name in ((w1, "w_top1"), (w2, "w_top2"), (w3, "w_top3"), (b1, "b_top1"), (b2, "b_top2")):
                        sp.dma_start(dst[:], a[name]).then_inc(mlp_loaded, 16)
            sp.wait_ge(y_done, 1)
            sp.dma_start(a["out"].rearrange("b o -> o b"), y[:]).then_inc(y_stored, 16)
            sp.wait_ge(y_stored, 16)

        @block.gpsimd
        def _(pool):
            pool.memset(ident[:], 0.0).then_inc(ident_zero, 1)
            pool.wait_ge(ident_zero, 1)
            pool.affine_select(out=ident[:], in_=ident[:], compare_op=ALU.not_equal, fill=1.0, base=0,
                               pattern=[[-1, P]], channel_multiplier=1).then_inc(ident_ready, 1)
            pool.wait_ge(ids_loaded, 16)

            def gather(n):
                if n >= ROW_BUFS:
                    pool.wait_ge(turn_done, n - ROW_BUFS + 1)
                for h in range(2):
                    f = 2 * n + h
                    for t in range(BT):
                        pool.indirect_dma_start(
                            out=rows[:, n % ROW_BUFS, t, h, :], out_offset=None, in_=tables[f],
                            in_offset=bass.IndirectOffsetOnAxis(ap=ids[:, t, f:f + 1].bitcast(U32), axis=0),
                        ).then_inc(rows_loaded[n % ROW_BUFS], 16)

            c = DVE_CHUNKS
            for n in range(NP):
                while c < NC and CU * c - POOL_W < FIRST[n] - POOL_X:
                    split_w_lo(pool, c, w_lo_pool)
                    c += 1
                gather(n)
            for c in range(c, NC):
                split_w_lo(pool, c, w_lo_pool)

        @block.scalar
        def _(act):
            def split_w_hi(c):
                act.wait_ge(raw_loaded[c % RAW_BUFS], 32 * (c // RAW_BUFS + 1))
                if c >= W_BUFS:
                    act.wait_ge(left_done, CU * (c - W_BUFS + 1))
                act.activation(w_hi[:, c % W_BUFS, :], w_raw[:, c % RAW_BUFS, :], ACT.Copy).then_inc(w_hi_done, 1)

            def copy_x(n):
                act.wait_ge(turn_done, n + 1)
                if n >= STACK_BUFS:
                    act.wait_ge(left_done, FIRST[n - 1])
                s = n % STACK_BUFS
                act.activation(stack[0:D, s, 0, :], turned[0:D, :], ACT.Copy)
                act.activation(stack[D:P, s, 1, :], turned[D:P, :], ACT.Copy)
                act.activation(xt[:, n, :], turned[:], ACT.Copy).then_inc(x_hi_done, 1)

            c = 0
            for n in range(NP):
                while c < chunks_by(n, LEAD_HI if c < DVE_CHUNKS else LEAD_HI_LATE):
                    split_w_hi(c)
                    c += 1
                copy_x(n)
            for c in range(c, NC):
                split_w_hi(c)
            act.wait_ge(mlp_loaded, 80)
            for k in (1, 3):
                act.wait_ge(l1_done, k + 1)
                act.activation(h1[:, k, :], h1_acc[k], ACT.Relu, bias=b1[:, k:k + 1]).then_inc(h1_odd, 1)

        @block.vector
        def _(dve):
            dve.memset(selector[:], 0.0).then_inc(selector_zero, 1)
            dve.memset(dense[:], 0.0).then_inc(dense_zero, 1)
            dve.wait_ge(selector_zero, 1)
            dve.memset(selector[0:D, 30:31], 1.0)
            dve.memset(selector[D:P, 31:32], 1.0).then_inc(selector_ready, 1)

            def split_x_lo(n, h):
                dve.wait_ge(x_hi_done, n + 1)
                s = n % STACK_BUFS
                own, free = (slice(0, D), slice(D, P)) if h == 0 else (slice(D, P), slice(0, D))
                dve.tensor_tensor(stack[free, s, h, :], xt[own, n, :], stack[own, s, h, :].bitcast(F32),
                                  ALU.subtract).then_inc(x_lo_done, 1)

            def multiply(u):
                n, m = UNITS[u]
                dve.wait_ge(left_done, u + 1)
                if u >= PROD_BUFS:
                    dve.wait_ge(reduce_done, (u - PROD_BUFS) // 2 + 1)
                other = xt[:, n - 1:n + 1, :] if m is None else xt[:, m:m + 1, :].to_broadcast([P, 2, B])
                dve.tensor_tensor(prod[:, u % PROD_BUFS, :, :], left[:, u % LEFT_BUFS, :, :], other,
                                  ALU.mult).then_inc(prod_done, 1)

            def copy_z(t):
                if t == 0:
                    dve.wait_ge(dense_loaded, 16 * NP)
                dve.wait_ge(reduce_done, UZ // 2 * (t + 1))
                dve.tensor_tensor(z[:, t, :], zsum[:], dense[:, t, :], ALU.add).then_inc(z_done, 1)

            c = 0
            x = 0
            for u in range(NU):
                while x < F and x_lo_at(x) <= u:
                    while c < min(chunks_by(x // 2, LEAD_LO), DVE_CHUNKS):
                        split_w_lo(dve, c, w_lo_dve)
                        c += 1
                    split_x_lo(x // 2, x % 2)
                    x += 1
                multiply(u)
                if u % UZ == 1 and u > UZ:
                    copy_z(u // UZ - 1)
            copy_z(NZ - 1)
            dve.wait_ge(mlp_loaded, 80)
            for k in (0, 2):
                dve.wait_ge(l1_done, k + 1)
                dve.tensor_scalar(h1[:, k, :], h1_acc[k], b1[:, k:k + 1], 0.0, ALU.add, ALU.max).then_inc(h1_even, 1)
            for k in range(H2 // P):
                dve.wait_ge(l2_done, k + 1)
                dve.tensor_scalar(h2[:, k, :], h2_acc[k], b2[:, k:k + 1], 0.0, ALU.add, ALU.max).then_inc(h2_done, 1)
            dve.wait_ge(l3_done, 1)
            dve.tensor_copy(y[:], y_acc).then_inc(y_done, 1)

        @block.tensor
        def _(pe):
            def transpose_x(n):
                pe.wait_ge(rows_loaded[n % ROW_BUFS], 16 * 2 * BT * (n // ROW_BUFS + 1))
                if n == 0:
                    pe.wait_ge(ident_ready, 1)
                else:
                    pe.wait_ge(x_hi_done, n)
                for t in range(BT):
                    mm = pe.transpose(turned[:, P * t:P * t + P],
                                      rows[:, n % ROW_BUFS, t, :, :].rearrange("p h d -> p (h d)"), ident[:])
                mm.then_inc(turn_done, 1)

            def left_products(u):
                n, m = UNITS[u]
                c = u // CU
                if u % CU == 0:
                    pe.wait_ge(w_hi_done, c + 1)
                    wait_w_lo(pe, c)
                if u == FIRST[n]:
                    pe.wait_ge(x_lo_done, 2 * (n + 1))
                if u >= LEFT_BUFS:
                    pe.wait_ge(prod_done, u - LEFT_BUFS + 1)
                for half in range(2):
                    j, _ = fields_of(u, half)
                    moving = stack[:, (j // 2) % STACK_BUFS, j % 2, :]
                    col = P * (2 * (u % CU) + half)
                    out = left[:, u % LEFT_BUFS, half, :]
                    pe.matmul(out, w_hi[:, c % W_BUFS, col:col + P], moving, start=True, stop=False)
                    mm = pe.matmul(out, w_lo[:, c % W_BUFS, col:col + P], moving, start=False, stop=True)
                mm.then_inc(left_done, 1)

            def reduce(pair):
                pe.wait_ge(prod_done, 2 * pair + 2)
                t = 2 * pair // UZ
                if 2 * pair % UZ == 0 and t:
                    pe.wait_ge(z_done, t)
                for u in (2 * pair, 2 * pair + 1):
                    for half in range(2):
                        _, g, q = z_place(u, half)
                        mm = pe.matmul(zsum[32 * g:32 * g + 32, :], selector[:, 30 - 2 * q:62 - 2 * q],
                                       prod[:, u % PROD_BUFS, half, :], start=(q == 0), stop=(q == 15),
                                       tile_position=(0, 32 * g))
                mm.then_inc(reduce_done, 1)

            def layer1(k, tiles, last=False):
                for t in tiles:
                    mm = pe.matmul(h1_acc[k], w1[:, t, P * k:P * k + P], z[:, t, :],
                                   start=(t == 0), stop=(t == NZ - 1))
                if last:
                    mm.then_inc(l1_done, 1)

            n = 0
            for u in range(NU):
                while n < NP and transposes_at(n) <= u:
                    transpose_x(n)
                    n += 1
                if u == 0:
                    pe.wait_ge(selector_ready, 1)
                left_products(u)
                if u % 2 and u > 1:
                    reduce(u // 2 - 1)
            pe.wait_ge(mlp_loaded, 80)
            pe.wait_ge(z_done, NZ - 1)
            pe.wait_ge(prod_done, NU - 2)
            layer1(0, range(NZ - 1))
            layer1(1, range(NZ - 1))
            reduce(NU // 2 - 1)
            layer1(2, range(NZ - 1))
            layer1(3, range(NZ - 1))
            pe.wait_ge(z_done, NZ)
            for k in range(H1 // P):
                layer1(k, [NZ - 1], last=True)
            for o in range(H2 // P):
                for k in range(H1 // P):
                    if o == 0:
                        pe.wait_ge(h1_odd if k % 2 else h1_even, k // 2 + 1)
                    mm = pe.matmul(h2_acc[o], w2[:, k, P * o:P * o + P], h1[:, k, :],
                                   start=(k == 0), stop=(k == H1 // P - 1))
                mm.then_inc(l2_done, 1)
            for k in range(H2 // P):
                pe.wait_ge(h2_done, k + 1)
                mm = pe.matmul(y_acc, w3[:, k:k + 1], h2[:, k, :], start=(k == 0), stop=(k == H2 // P - 1))
            mm.then_inc(l3_done, 1)


def kernel(**inputs):
    import concourse.bacc as bacc
    from concourse.bass_utils import run_bass_kernel_spmd

    w = np.asarray(inputs["L0_rec_W"])
    order = [pair_index(i, fields_of(u, half)[0]) if i is not None else len(w)
             for u in range(NU) for half in range(2) for i in fields_of(u, half)[1]]
    padded = np.concatenate([w.transpose(0, 2, 1), np.zeros((1, D, D), w.dtype)])
    pair_w = padded[np.array(order)].reshape(NC, 4 * CU, D, D).transpose(0, 2, 1, 3).reshape(NC, D, CC)

    w_top1 = np.asarray(inputs["W_top1"])
    row_of = np.zeros((P, NZ), np.int64)
    for u in range(NU):
        for half in range(2):
            t, g, q = z_place(u, half)
            j, outs = fields_of(u, half)
            for o, i in enumerate(outs):
                row_of[32 * g + 2 * q + o, t] = len(w) + j // 2 if i is None else pair_index(i, j)

    arrays = {f"tbl_{f}": np.asarray(inputs[f"tbl_{f}"]) for f in range(F)}
    arrays["ids"] = np.asarray(inputs["ids"])
    arrays["pair_w"] = pair_w
    arrays["dense_t"] = np.asarray(inputs["dense_ctx"]).T
    arrays["w_top1"] = w_top1[row_of]
    arrays["w_top2"] = np.asarray(inputs["W_top2"]).reshape(H1 // P, P, H2).transpose(1, 0, 2)
    arrays["w_top3"] = np.asarray(inputs["W_top3"]).reshape(H2 // P, P).T
    arrays["b_top1"] = np.asarray(inputs["b_top1"]).reshape(H1 // P, P).T
    arrays["b_top2"] = np.asarray(inputs["b_top2"]).reshape(H2 // P, P).T
    arrays = {k: np.ascontiguousarray(v) for k, v in arrays.items()}

    nc = bacc.Bacc("TRN2", target_bir_lowering=False, num_devices=1)
    aps = {k: nc.dram_tensor(f"{k}_dram", v.shape, mybir.dt.from_np(v.dtype), kind="ExternalInput").ap()
           for k, v in arrays.items()}
    aps["out"] = nc.dram_tensor("out_dram", (B, 1), F32, kind="ExternalOutput").ap()
    build(nc, aps)
    arrays = {f"{k}_dram": v for k, v in arrays.items()}
    return run_bass_kernel_spmd(nc, [arrays], core_ids=[0]).results[0]["out_dram"]
```

```python
from contextlib import ExitStack

import numpy as np

import concourse.bass as bass
from concourse import mybir

ALU = mybir.AluOpType
ACT = mybir.ActivationFunctionType
F32 = mybir.dt.float32
F32R = mybir.dt.float32r
I32 = mybir.dt.int32
U32 = mybir.dt.uint32

B, F, D = 512, 32, 64
P = 128
H1, H2 = 512, 256
BT = B // P
NP = F // 2
BANK = 512

ONE_HOT = [4, 6, 7, 14]
TABLE_ROWS = 1000
HC = 8
HP = TABLE_ROWS // HC
FIELD_AT = ONE_HOT + [f for f in range(F) if f not in ONE_HOT]
NO = len(ONE_HOT)
OP = NO // 2

UNITS = []
FIRST = []
for _n in range(NP):
    FIRST.append(len(UNITS))
    UNITS += [(_n, _m) for _m in range(_n)]
    if _n % 2:
        UNITS.append((_n, None))
NU = len(UNITS)
CU = 4
NC = NU // CU
CC = CU * 2 * P
UZ = NU // BT
NZ = NU // UZ

LEFT_BUFS = 3
PROD_BUFS = 4
RAW_BUFS = 3
W_BUFS = 9
DVE_PARTS = [7, 7, 7, 7]
BY_DVE = [(i, c) for i in range(NO) for c in range(HC) if c < DVE_PARTS[i]]
BY_ACT = [(i, c) for i in range(NO) for c in range(HC) if c >= DVE_PARTS[i]]
HOT_BUFS = 3
STACK_BUFS = 3
ROW_BUFS = 4

AHEAD = [0, 0, 2, 2, 3, 3, 3, 3, 6, 5, 6, 6, 6, 6, 6, 6]
LO_AFTER = [1, 1, 1, 0, 1, 1, 1, 1, 3, 2, 2, 2, 1, 2, 2, 2]
ODD_AFTER = [0, 0, 0, 0, 0, 0, 0, 0, 1, 1, 1, 0, 1, 1, 1, 1]
HI_BY = [3, 3, 4, 4, 6, 8, 10, 11, 12, 14, 17, 19, 22, 26, 29, 32]
LO_AHEAD = [0, 5, 12, 8, 8, 8, 8, 8, 8]
DVE_CHUNKS = len(LO_AHEAD)
POOL_BY = [0, 0, 0, 0, 0, 0, 0, 0, 0, 2, 2, 5, 7, 11, 14, 18]
DENSE_ZERO = 8
MLP_LOAD = 13


def fields_of(u, half):
    n, m = UNITS[u]
    if m is None:
        k = n - 1 + half
        return 2 * k + 1, (2 * k, None)
    return 2 * n + half, (2 * m, 2 * m + 1)


def pair_index(i, j):
    i, j = min(i, j), max(i, j)
    return i * F - i * (i + 1) // 2 + (j - i - 1)


def z_place(u, half):
    block = 2 * (u % UZ) + half
    return u // UZ, block % 4, block // 4


def transposes_at(n):
    return FIRST[n] - AHEAD[n]


def x_lo_at(x):
    n, h = x // 2, x % 2
    return min(transposes_at(n) + LO_AFTER[n] + ODD_AFTER[n] * h, FIRST[n])


def build(nc, a):
    tables = [a[f"tbl_{f}"] for f in FIELD_AT]
    ctx = ExitStack()
    with ctx:
        def sb(name, shape, dt=F32):
            return ctx.enter_context(nc.sbuf_tensor(name, shape, dt))

        def sem(name):
            return ctx.enter_context(nc.semaphore(name))

        ident = sb("ident", [P, P])
        selector = sb("selector", [P, 62])
        ids = sb("ids", [P, BT, F], I32)
        row_no = sb("row_no", [HP, HC])
        minus_row = sb("minus_row", [HP, HC])
        table_parts = sb("table_parts", [HP, NO, HC, 2, D], F32R)
        hot = sb("hot", [HP, HOT_BUFS, B], F32R)
        merge_raw = sb("merge_raw", [P, 3, D])
        merge = sb("merge", [P, 3, D], F32R)
        rows = sb("rows", [P, ROW_BUFS, BT, 2, D])
        xt = sb("xt", [P, NP, B])
        stack = sb("stack", [P, STACK_BUFS, 2, B], F32R)
        w_raw = sb("w_raw", [P, RAW_BUFS, CC])
        w_hi = sb("w_hi", [P, W_BUFS, CC], F32R)
        w_lo = sb("w_lo", [P, W_BUFS, CC], F32R)
        prod = sb("prod", [P, PROD_BUFS, 2, B])
        dense = sb("dense", [P, NZ, B])
        z = sb("z", [P, NZ, B])
        w1 = sb("w1", [P, NZ, H1])
        w2 = sb("w2", [P, H1 // P, H2])
        w3 = sb("w3", [P, H2 // P])
        b1 = sb("b1", [P, H1 // P])
        b2 = sb("b2", [P, H2 // P])
        table = z[:HP, :, :].rearrange("p i (c d) -> p i c d", c=HC)
        hot_ids = dense[:HP, :, :].bitcast(I32)
        act_hot = w_hi[:HP, W_BUFS - (len(BY_ACT) + 1) // 2:, :].rearrange("p w (k b) -> p (w k) b", b=B)
        distance = prod[:HP, 0, :, :]
        h1 = xt[:, :H1 // P, :]
        h2 = xt[:, H1 // P:(H1 + H2) // P, :]
        y = xt[0:1, (H1 + H2) // P, :]

        left = ctx.enter_context(nc.psum_tensor("left", [P, LEFT_BUFS, 2, BANK], F32))
        turned = ctx.enter_context(nc.psum_tensor("turned", [P, BANK], F32))
        zsum = ctx.enter_context(nc.psum_tensor("zsum", [P, BANK], F32))
        found = [left[:, f // 2, f % 2, :] for f in range(NO)]
        h1_acc = [left[:, 2, 0, :], left[:, 2, 1, :], left[:, 0, 0, :], left[:, 0, 1, :]]
        h2_acc = [left[:, 1, 0, :], left[:, 1, 1, :]]
        y_acc = turned[0:1, :]

        ids_loaded = sem("ids_loaded")
        hot_ids_loaded = [sem(f"hot_ids_loaded{i}") for i in range(NO)]
        table_loaded = [sem(f"table_loaded{i}") for i in range(NO)]
        merge_zero = sem("merge_zero")
        merge_half = sem("merge_half")
        merge_raw_ready = sem("merge_raw_ready")
        merge_ready = sem("merge_ready")
        row_no_ready = sem("row_no_ready")
        table_hi_done = sem("table_hi_done")
        table_lo_done = sem("table_lo_done")
        minus_row_ready = sem("minus_row_ready")
        hot_ready = sem("hot_ready")
        distance_ready = sem("distance_ready")
        act_hot_ready = sem("act_hot_ready")
        hot_used = sem("hot_used")
        found_copied = sem("found_copied")
        merge_done = sem("merge_done")
        raw_loaded = [sem(f"raw_loaded{i}") for i in range(RAW_BUFS)]
        mlp_loaded = sem("mlp_loaded")
        dense_loaded = sem("dense_loaded")
        rows_loaded = [sem(f"rows_loaded{i}") for i in range(ROW_BUFS)]
        y_stored = sem("y_stored")
        ident_zero = sem("ident_zero")
        ident_ready = sem("ident_ready")
        selector_zero = sem("selector_zero")
        selector_ready = sem("selector_ready")
        dense_zero = sem("dense_zero")
        turn_done = sem("turn_done")
        x_hi_done = sem("x_hi_done")
        x_lo_done = sem("x_lo_done")
        w_hi_done = sem("w_hi_done")
        w_lo_dve = sem("w_lo_dve")
        w_lo_pool = sem("w_lo_pool")
        left_done = sem("left_done")
        prod_done = sem("prod_done")
        reduce_done = sem("reduce_done")
        z_done = sem("z_done")
        l1_done = sem("l1_done")
        h1_even = sem("h1_even")
        h1_odd = sem("h1_odd")
        l2_done = sem("l2_done")
        h2_done = sem("h2_done")
        l3_done = sem("l3_done")
        y_done = sem("y_done")

        def wait_w_lo(eng, c):
            if c < DVE_CHUNKS:
                eng.wait_ge(w_lo_dve, c + 1)
            else:
                eng.wait_ge(w_lo_pool, c - DVE_CHUNKS + 1)

        def split_w_lo(eng, c, done):
            eng.wait_ge(w_hi_done, c + 1)
            if c >= W_BUFS:
                eng.wait_ge(left_done, CU * (c - W_BUFS + 1))
            eng.tensor_tensor(w_lo[:, c % W_BUFS, :], w_raw[:, c % RAW_BUFS, :],
                              w_hi[:, c % W_BUFS, :].bitcast(F32), ALU.subtract).then_inc(done, 1)

        block = ctx.enter_context(nc.Block())

        @block.sync
        def _(sp):
            sp.dma_start(ids[:], a["ids"].rearrange("(t p) f -> p t f", p=P)).then_inc(ids_loaded, 16)
            for i in range(NO):
                sp.dma_start(table[:, i, :, :],
                             tables[i].rearrange("(p c) d -> p c d", c=HC)).then_inc(table_loaded[i], 16)
                sp.dma_start(hot_ids[:, i, :], a["hot_ids"][i:i + 1, :].to_broadcast([HP, B])
                             ).then_inc(hot_ids_loaded[i], 16)
            for c in range(NC):
                if c >= RAW_BUFS:
                    wait_w_lo(sp, c - RAW_BUFS)
                for half in range(2):
                    sp.dma_start(w_raw[D * half:D * half + D, c % RAW_BUFS, :],
                                 a["pair_w"][c]).then_inc(raw_loaded[c % RAW_BUFS], 16)
                if c == MLP_LOAD:
                    sp.wait_ge(dense_zero, 1)
                    for k in range(NP):
                        t, g, q = z_place(FIRST[k | 1] + (k | 1), k % 2)
                        r = 32 * g + 2 * q + 1
                        sp.dma_start(dense[r:r + 1, t, :], a["dense_t"][k:k + 1, :]).then_inc(dense_loaded, 16)
                    for dst, name in ((w1, "w_top1"), (w2, "w_top2"), (w3, "w_top3"), (b1, "b_top1"), (b2, "b_top2")):
                        sp.dma_start(dst[:], a[name]).then_inc(mlp_loaded, 16)
            sp.wait_ge(y_done, 1)
            sp.dma_start(a["out"].rearrange("b o -> o b"), y).then_inc(y_stored, 16)
            sp.wait_ge(y_stored, 16)

        @block.gpsimd
        def _(pool):
            pool.memset(ident[:], 0.0).then_inc(ident_zero, 1)
            pool.wait_ge(ident_zero, 1)
            pool.affine_select(out=ident[:], in_=ident[:], compare_op=ALU.not_equal, fill=1.0, base=0,
                               pattern=[[-1, P]], channel_multiplier=1).then_inc(ident_ready, 1)
            pool.iota(row_no[:], pattern=[[1, HC]], base=0, channel_multiplier=HC,
                      allow_small_or_imprecise_dtypes=True).then_inc(row_no_ready, 1)
            pool.iota(minus_row[:], pattern=[[-1, HC]], base=0, channel_multiplier=-HC,
                      allow_small_or_imprecise_dtypes=True).then_inc(minus_row_ready, 1)
            pool.memset(merge_raw[:], 0.0).then_inc(merge_zero, 1)
            pool.wait_ge(merge_zero, 1)
            pool.affine_select(out=merge_raw[:, 1, :], in_=merge_raw[:, 1, :], compare_op=ALU.not_equal, fill=1.0,
                               base=0, pattern=[[-1, D]], channel_multiplier=1).then_inc(merge_half, 1)
            pool.wait_ge(merge_half, 1)
            pool.affine_select(out=merge_raw[:, 1, :], in_=merge_raw[:, 1, :], compare_op=ALU.not_equal, fill=1.0,
                               base=-D, pattern=[[-1, D]], channel_multiplier=1).then_inc(merge_raw_ready, 1)
            pool.wait_ge(ids_loaded, 16)

            def gather(n):
                if n >= OP + ROW_BUFS:
                    pool.wait_ge(turn_done, n - OP - ROW_BUFS + 1)
                for h in range(2):
                    f = FIELD_AT[2 * n + h]
                    for t in range(BT):
                        pool.indirect_dma_start(
                            out=rows[:, n % ROW_BUFS, t, h, :], out_offset=None,
                            in_=tables[2 * n + h],
                            in_offset=bass.IndirectOffsetOnAxis(ap=ids[:, t, f:f + 1].bitcast(U32), axis=0),
                        ).then_inc(rows_loaded[n % ROW_BUFS], 16)

            c = DVE_CHUNKS
            for n in range(OP, NP):
                while c < DVE_CHUNKS + POOL_BY[n]:
                    split_w_lo(pool, c, w_lo_pool)
                    c += 1
                if n == DENSE_ZERO:
                    pool.wait_ge(hot_used, HC * NO)
                    pool.memset(dense[:], 0.0).then_inc(dense_zero, 1)
                gather(n)
            for c in range(c, NC):
                split_w_lo(pool, c, w_lo_pool)

        @block.scalar
        def _(act):
            def split_w_hi(c):
                act.wait_ge(raw_loaded[c % RAW_BUFS], 32 * (c // RAW_BUFS + 1))
                if c >= W_BUFS:
                    act.wait_ge(left_done, CU * (c - W_BUFS + 1))
                act.activation(w_hi[:, c % W_BUFS, :], w_raw[:, c % RAW_BUFS, :], ACT.Copy).then_inc(w_hi_done, 1)

            def split_table_hi(i):
                act.wait_ge(table_loaded[i], 16)
                act.activation(table_parts[:, i, :, 0, :], table[:, i, :, :], ACT.Copy).then_inc(table_hi_done, 1)

            def measure(k):
                i, c = BY_ACT[k]
                if k == 0:
                    act.wait_ge(minus_row_ready, 1)
                act.wait_ge(hot_ids_loaded[i], 16)
                if k >= 2:
                    act.wait_ge(act_hot_ready, k - 1)
                act.activation(distance[:, k % 2, :], hot_ids[:, i, :], ACT.Abs,
                               bias=minus_row[:, c:c + 1]).then_inc(distance_ready, 1)

            def compare(k):
                act.wait_ge(distance_ready, k + 1)
                act.activation(act_hot[:, k, :], distance[:, k % 2, :], ACT.Relu,
                               bias=1.0, scale=-1.0).then_inc(act_hot_ready, 1)

            def copy_found(n):
                for h in range(2):
                    act.wait_ge(hot_used, HC * (2 * n + h + 1))
                    act.activation(stack[:, n, h, :], found[2 * n + h], ACT.Copy).then_inc(found_copied, 1)
                act.wait_ge(merge_done, n + 1)
                act.activation(xt[:, n, :], turned[:], ACT.Copy).then_inc(x_hi_done, 1)

            def copy_x(n):
                act.wait_ge(turn_done, n - OP + 1)
                if n >= STACK_BUFS:
                    act.wait_ge(left_done, FIRST[n - 1])
                s = n % STACK_BUFS
                act.activation(stack[0:D, s, 0, :], turned[0:D, :], ACT.Copy)
                act.activation(stack[D:P, s, 1, :], turned[D:P, :], ACT.Copy)
                act.activation(xt[:, n, :], turned[:], ACT.Copy).then_inc(x_hi_done, 1)

            act.wait_ge(merge_raw_ready, 1)
            act.activation(merge[:], merge_raw[:], ACT.Copy).then_inc(merge_ready, 1)
            for i in range(NO):
                split_table_hi(i)
                if i:
                    compare(i - 1)
                measure(i)
            for k in range(NO - 1, len(BY_ACT)):
                if k + 1 < len(BY_ACT):
                    measure(k + 1)
                compare(k)
            c = 0
            for n in range(NP):
                if n < OP:
                    copy_found(n)
                else:
                    copy_x(n)
                while c < HI_BY[n]:
                    split_w_hi(c)
                    c += 1
            for c in range(c, NC):
                split_w_hi(c)
            act.wait_ge(mlp_loaded, 80)
            for k in (1, 3):
                act.wait_ge(l1_done, k + 1)
                act.activation(h1[:, k, :], h1_acc[k], ACT.Relu, bias=b1[:, k:k + 1]).then_inc(h1_odd, 1)

        @block.vector
        def _(dve):
            dve.memset(selector[:], 0.0).then_inc(selector_zero, 1)
            dve.wait_ge(selector_zero, 1)
            dve.memset(selector[0:D, 30:31], 1.0)
            dve.memset(selector[D:P, 31:32], 1.0).then_inc(selector_ready, 1)

            def one_hots(i):
                dve.wait_ge(table_hi_done, i + 1)
                dve.tensor_tensor(table_parts[:, i, :, 1, :], table[:, i, :, :],
                                  table_parts[:, i, :, 0, :].bitcast(F32), ALU.subtract).then_inc(table_lo_done, 1)
                if i == 0:
                    dve.wait_ge(row_no_ready, 1)
                dve.wait_ge(hot_ids_loaded[i], 16)
                for c in range(DVE_PARTS[i]):
                    k = BY_DVE.index((i, c))
                    if k >= HOT_BUFS:
                        old_i, old_c = BY_DVE[k - HOT_BUFS]
                        dve.wait_ge(hot_used, HC * old_i + old_c + 1)
                    dve.tensor_scalar(hot[:, k % HOT_BUFS, :], hot_ids[:, i, :], row_no[:, c:c + 1], None,
                                      ALU.is_equal).then_inc(hot_ready, 1)

            def split_x_lo(n, h):
                dve.wait_ge(x_hi_done, n + 1)
                s = n % STACK_BUFS
                own, free = (slice(0, D), slice(D, P)) if h == 0 else (slice(D, P), slice(0, D))
                dve.tensor_tensor(stack[free, s, h, :], xt[own, n, :], stack[own, s, h, :].bitcast(F32),
                                  ALU.subtract).then_inc(x_lo_done, 1)

            def multiply(u):
                n, m = UNITS[u]
                if n < OP:
                    dve.wait_ge(x_hi_done, n + 1)
                dve.wait_ge(left_done, u + 1)
                if u >= PROD_BUFS:
                    dve.wait_ge(reduce_done, (u - PROD_BUFS) // 2 + 1)
                other = xt[:, n - 1:n + 1, :] if m is None else xt[:, m:m + 1, :].to_broadcast([P, 2, B])
                dve.tensor_tensor(prod[:, u % PROD_BUFS, :, :], left[:, u % LEFT_BUFS, :, :], other,
                                  ALU.mult).then_inc(prod_done, 1)

            def copy_z(t):
                if t == 0:
                    dve.wait_ge(dense_loaded, 16 * NP)
                dve.wait_ge(reduce_done, UZ // 2 * (t + 1))
                dve.tensor_tensor(z[:, t, :], zsum[:], dense[:, t, :], ALU.add).then_inc(z_done, 1)

            for i in range(NO):
                one_hots(i)
            c = 0
            x = NO
            for u in range(NU):
                while x < F and x_lo_at(x) <= u:
                    split_x_lo(x // 2, x % 2)
                    x += 1
                while c < DVE_CHUNKS and CU * c - LO_AHEAD[c] <= u:
                    split_w_lo(dve, c, w_lo_dve)
                    c += 1
                multiply(u)
                if u % UZ == 1 and u > UZ:
                    copy_z(u // UZ - 1)
            copy_z(NZ - 1)
            dve.wait_ge(mlp_loaded, 80)
            for k in (0, 2):
                dve.wait_ge(l1_done, k + 1)
                dve.tensor_scalar(h1[:, k, :], h1_acc[k], b1[:, k:k + 1], 0.0, ALU.add, ALU.max).then_inc(h1_even, 1)
            for k in range(H2 // P):
                dve.wait_ge(l2_done, k + 1)
                dve.tensor_scalar(h2[:, k, :], h2_acc[k], b2[:, k:k + 1], 0.0, ALU.add, ALU.max).then_inc(h2_done, 1)
            dve.wait_ge(l3_done, 1)
            dve.tensor_copy(y, y_acc).then_inc(y_done, 1)

        @block.tensor
        def _(pe):
            def look_up(i):
                pe.wait_ge(table_lo_done, i + 1)
                for c in range(HC):
                    if c < DVE_PARTS[i]:
                        k = BY_DVE.index((i, c))
                        pe.wait_ge(hot_ready, k + 1)
                        part = hot[:, k % HOT_BUFS, :]
                    else:
                        k = BY_ACT.index((i, c))
                        pe.wait_ge(act_hot_ready, k + 1)
                        part = act_hot[:, k, :]
                    pe.matmul(found[i], table_parts[:, i, c, :, :].rearrange("p h d -> p (h d)"), part, start=(c == 0), stop=(c == HC - 1)).then_inc(hot_used, 1)

            def merge_x(n):
                if n:
                    pe.wait_ge(x_hi_done, n)
                else:
                    pe.wait_ge(merge_ready, 1)
                for h in range(2):
                    pe.wait_ge(found_copied, 2 * n + h + 1)
                    mm = pe.matmul(turned[:], merge[:, 1 - h:3 - h, :].rearrange("p a d -> p (a d)"),
                                   stack[:, n, h, :], start=(h == 0), stop=(h == 1))
                mm.then_inc(merge_done, 1)

            def transpose_x(n):
                pe.wait_ge(rows_loaded[n % ROW_BUFS], 16 * 2 * BT * ((n - OP) // ROW_BUFS + 1))
                if n == OP:
                    pe.wait_ge(ident_ready, 1)
                pe.wait_ge(x_hi_done, n)
                for t in range(BT):
                    mm = pe.transpose(turned[:, P * t:P * t + P],
                                      rows[:, n % ROW_BUFS, t, :, :].rearrange("p h d -> p (h d)"), ident[:])
                mm.then_inc(turn_done, 1)

            def left_products(u):
                n, m = UNITS[u]
                c = u // CU
                if u % CU == 0:
                    pe.wait_ge(w_hi_done, c + 1)
                    wait_w_lo(pe, c)
                if u == FIRST[n]:
                    if n < OP:
                        pe.wait_ge(found_copied, NO)
                    else:
                        pe.wait_ge(x_lo_done, 2 * (n + 1 - OP))
                if u >= LEFT_BUFS:
                    pe.wait_ge(prod_done, u - LEFT_BUFS + 1)
                for half in range(2):
                    j, _ = fields_of(u, half)
                    moving = stack[:, (j // 2) % STACK_BUFS, j % 2, :]
                    col = P * (2 * (u % CU) + half)
                    out = left[:, u % LEFT_BUFS, half, :]
                    pe.matmul(out, w_hi[:, c % W_BUFS, col:col + P], moving, start=True, stop=False)
                    mm = pe.matmul(out, w_lo[:, c % W_BUFS, col:col + P], moving, start=False, stop=True)
                mm.then_inc(left_done, 1)

            def reduce(pair):
                pe.wait_ge(prod_done, 2 * pair + 2)
                t = 2 * pair // UZ
                if 2 * pair % UZ == 0 and t:
                    pe.wait_ge(z_done, t)
                for u in (2 * pair, 2 * pair + 1):
                    for half in range(2):
                        _, g, q = z_place(u, half)
                        mm = pe.matmul(zsum[32 * g:32 * g + 32, :], selector[:, 30 - 2 * q:62 - 2 * q],
                                       prod[:, u % PROD_BUFS, half, :], start=(q == 0), stop=(q == 15),
                                       tile_position=(0, 32 * g))
                mm.then_inc(reduce_done, 1)

            def layer1(k, tiles, last=False):
                for t in tiles:
                    mm = pe.matmul(h1_acc[k], w1[:, t, P * k:P * k + P], z[:, t, :],
                                   start=(t == 0), stop=(t == NZ - 1))
                if last:
                    mm.then_inc(l1_done, 1)

            for i in range(NO):
                look_up(i)
                if i % 2:
                    merge_x(i // 2)
            n = OP
            for u in range(NU):
                while n < NP and transposes_at(n) <= u:
                    transpose_x(n)
                    n += 1
                if u == 0:
                    pe.wait_ge(selector_ready, 1)
                left_products(u)
                if u % 2 and u > 1:
                    reduce(u // 2 - 1)
            pe.wait_ge(mlp_loaded, 80)
            pe.wait_ge(z_done, NZ - 1)
            pe.wait_ge(prod_done, NU - 2)
            layer1(0, range(NZ - 1))
            layer1(1, range(NZ - 1))
            reduce(NU // 2 - 1)
            layer1(2, range(NZ - 1))
            layer1(3, range(NZ - 1))
            pe.wait_ge(z_done, NZ)
            for k in range(H1 // P):
                layer1(k, [NZ - 1], last=True)
            for o in range(H2 // P):
                for k in range(H1 // P):
                    if o == 0:
                        pe.wait_ge(h1_odd if k % 2 else h1_even, k // 2 + 1)
                    mm = pe.matmul(h2_acc[o], w2[:, k, P * o:P * o + P], h1[:, k, :],
                                   start=(k == 0), stop=(k == H1 // P - 1))
                mm.then_inc(l2_done, 1)
            for k in range(H2 // P):
                pe.wait_ge(h2_done, k + 1)
                mm = pe.matmul(y_acc, w3[:, k:k + 1], h2[:, k, :], start=(k == 0), stop=(k == H2 // P - 1))
            mm.then_inc(l3_done, 1)


def kernel(**inputs):
    import concourse.bacc as bacc
    from concourse.bass_utils import run_bass_kernel_spmd

    w = np.asarray(inputs["L0_rec_W"])
    pair_w = []
    for u in range(NU):
        for half in range(2):
            j, outs = fields_of(u, half)
            for i in outs:
                if i is None:
                    pair_w.append(np.zeros((D, D), w.dtype))
                else:
                    fi, fj = FIELD_AT[i], FIELD_AT[j]
                    pair_w.append(w[pair_index(fi, fj)].T if fi < fj else w[pair_index(fi, fj)])
    pair_w = np.stack(pair_w).reshape(NC, 4 * CU, D, D).transpose(0, 2, 1, 3).reshape(NC, D, CC)

    w_top1 = np.asarray(inputs["W_top1"])
    row_of = np.zeros((P, NZ), np.int64)
    for u in range(NU):
        for half in range(2):
            t, g, q = z_place(u, half)
            j, outs = fields_of(u, half)
            for o, i in enumerate(outs):
                row_of[32 * g + 2 * q + o, t] = (len(w) + j // 2 if i is None else
                                                  pair_index(FIELD_AT[i], FIELD_AT[j]))

    arrays = {f"tbl_{f}": np.asarray(inputs[f"tbl_{f}"]) for f in range(F)}
    arrays["ids"] = np.asarray(inputs["ids"])
    arrays["hot_ids"] = arrays["ids"].T[ONE_HOT]
    arrays["pair_w"] = pair_w
    arrays["dense_t"] = np.asarray(inputs["dense_ctx"]).T
    arrays["w_top1"] = w_top1[row_of]
    arrays["w_top2"] = np.asarray(inputs["W_top2"]).reshape(H1 // P, P, H2).transpose(1, 0, 2)
    arrays["w_top3"] = np.asarray(inputs["W_top3"]).reshape(H2 // P, P).T
    arrays["b_top1"] = np.asarray(inputs["b_top1"]).reshape(H1 // P, P).T
    arrays["b_top2"] = np.asarray(inputs["b_top2"]).reshape(H2 // P, P).T
    arrays = {k: np.ascontiguousarray(v) for k, v in arrays.items()}

    nc = bacc.Bacc("TRN2", target_bir_lowering=False, num_devices=1)
    aps = {k: nc.dram_tensor(f"{k}_dram", v.shape, mybir.dt.from_np(v.dtype), kind="ExternalInput").ap()
           for k, v in arrays.items()}
    aps["out"] = nc.dram_tensor("out_dram", (B, 1), F32, kind="ExternalOutput").ap()
    build(nc, aps)
    arrays = {f"{k}_dram": v for k, v in arrays.items()}
    return run_bass_kernel_spmd(nc, [arrays], core_ids=[0]).results[0]["out_dram"]
```
